# Optimizing a Trainium2 kernel written in Bass

```python
import numpy as np
import jax
import jax.numpy as jnp

def _softmax(x, axis=-1):
    return jax.nn.softmax(x, axis=axis)

def _gelu(x):
    return jax.nn.gelu(x, approximate=True)

def _silu(x):
    return jax.nn.silu(x)

def _sigmoid(x):
    return jax.nn.sigmoid(x)

def _layernorm(x, axis=-1, eps=1e-05):
    m = jnp.mean(x, axis=axis, keepdims=True)
    v = jnp.var(x, axis=axis, keepdims=True)
    return (x - m) / jnp.sqrt(v + eps)

def _scatter_add(tgt, idx, src, axis=0):
    return tgt.at[idx].add(src)

def _segment_sum(src, seg, n):
    return jax.ops.segment_sum(src, seg, n)
kernel_name = 'mk_prb_d1_jaxref_r8_639fe7'

def setup_inputs(seed: int=0):
    np.random.seed(seed)
    _w = jnp.asarray

    def _L0_attn_setup():
        import jax, jax.numpy as jnp
        import numpy as np
        _A = np.array([[1, 1, 1, 0, 1, 1, 1, 0, 0, 0, 1, 1], [1, 1, 0, 1, 1, 1, 0, 0, 0, 1, 1, 0], [1, 0, 1, 1, 1, 0, 0, 0, 1, 1, 0, 1], [0, 1, 1, 1, 0, 0, 0, 1, 1, 0, 1, 1], [0, 0, 0, 0, 1, 1, 1, 1, 1, 1, 1, 1], [1, 1, 1, 1, 0, 0, 0, 0, 0, 0, 0, 0], [0, 0, 0, 0, 1, 1, 1, 1, 0, 0, 0, 0], [1, 1, 0, 0, 1, 1, 0, 0, 1, 1, 0, 0], [1, 0, 1, 0, 1, 0, 1, 0, 1, 0, 1, 0], [0, 1, 0, 1, 0, 1, 0, 1, 0, 1, 0, 1], [1, 0, 0, 1, 1, 0, 0, 1, 1, 0, 0, 1], [0, 1, 1, 0, 0, 1, 1, 0, 0, 1, 1, 0]], dtype=np.float32)
        _H = jnp.asarray(np.concatenate([_A.T, np.eye(12, dtype=np.float32)], axis=1))

        def _fractal_dimension(x):
            s = x.reshape(-1)
            sn = (s - s.min()) / (s.max() - s.min() + 1e-10)
            counts = []
            for sc in (2, 4, 8, 16, 32):
                blk = sn[:sc * sc]
                counts.append(jnp.maximum(jnp.sum(blk > blk.mean()).astype(jnp.float32), 1.0))
            lx = jnp.log(jnp.array([2.0, 4.0, 8.0, 16.0, 32.0], dtype=jnp.float32))
            ly = jnp.log(jnp.stack(counts))
            n = jnp.float32(5.0)
            num = n * jnp.sum(lx * ly) - jnp.sum(lx) * jnp.sum(ly)
            den = n * jnp.sum(lx * lx) - jnp.sum(lx) ** 2
            return jnp.clip(-num / den, 1.0, 2.0)

        def _wave_filter(D, d):
            k = jnp.fft.fftfreq(d).astype(jnp.float32)
            ka = jnp.abs(k) + 1e-08
            omega = 1.0 + 0.2 * D
            a = 1.0 + 0.5 * D
            b = 0.1 * D
            real = jnp.sin(omega * D + a * ka)
            phase = omega * D - ka + b * ka ** 2
            return real * jnp.exp(1j * phase)

        def _golay_correct(bits):
            syn = (bits @ _H.T > 0.5).astype(jnp.float32)
            w = syn.sum(-1)
            _, idx = jax.lax.top_k(syn, 3)
            take = (jnp.arange(3)[None, :] < jnp.minimum(w, 3.0)[:, None]).astype(jnp.float32)
            pattern = (jax.nn.one_hot(idx, 24, dtype=jnp.float32) * take[..., None]).sum(axis=1)
            do_fix = ((w > 0) & (w <= 3))[:, None]
            return jnp.where(do_fix, jnp.mod(bits + pattern, 2.0), bits)
        key = jax.random.key(seed)
        k1, k2, k3 = jax.random.split(key, 3)
        B, S, E = (8, 256, 128)
        x = jax.random.normal(k1, (B, S, E), dtype=jnp.float32)
        W_el = jax.random.normal(k2, (E, 24), dtype=jnp.float32) * 0.02
        b_el = jnp.zeros((24,), dtype=jnp.float32)
        W_le = jax.random.normal(k3, (24, E), dtype=jnp.float32) * 0.02
        b_le = jnp.zeros((E,), dtype=jnp.float32)
        return {'x': x, 'W_el': W_el, 'b_el': b_el, 'W_le': W_le, 'b_le': b_le}
    _L0_attn_in = _L0_attn_setup()

    def _L0_ffn_setup():
        import jax, jax.numpy as jnp
        import numpy as np
        B, N, C, F, E, K = (2, 256, 128, 512, 8, 2)
        key = jax.random.key(seed)
        k = jax.random.split(key, 6)
        xavier1 = float(np.sqrt(6.0 / (C + F)))
        xavier2 = float(np.sqrt(6.0 / (F + C)))
        return {'x': jax.random.normal(k[0], (B, N, C), dtype=jnp.float32), 'router_w': jax.random.normal(k[1], (E, C), dtype=jnp.float32) * 0.01, 'w1': jax.random.uniform(k[2], (E, F, C), dtype=jnp.float32, minval=-xavier1, maxval=xavier1), 'b1': jnp.zeros((E, F), dtype=jnp.float32), 'w2': jax.random.uniform(k[3], (E, C, F), dtype=jnp.float32, minval=-xavier2, maxval=xavier2), 'b2': jnp.zeros((E, C), dtype=jnp.float32)}
    _L0_ffn_in = _L0_ffn_setup()
    _d = {'L0_attn_x': _L0_attn_in['x'], 'L0_attn_W_el': _L0_attn_in['W_el'], 'L0_attn_b_el': _L0_attn_in['b_el'], 'L0_attn_W_le': _L0_attn_in['W_le'], 'L0_attn_b_le': _L0_attn_in['b_le'], 'L0_ffn_router_w': _L0_ffn_in['router_w'], 'L0_ffn_w1': _L0_ffn_in['w1'], 'L0_ffn_b1': _L0_ffn_in['b1'], 'L0_ffn_w2': _L0_ffn_in['w2'], 'L0_ffn_b2': _L0_ffn_in['b2']}
    _x0 = _d['L0_attn_x']
    _d['L0_attn_x'] = jax.random.normal(jax.random.fold_in(jax.random.key(seed), 1), (32, 256, 128), dtype=_x0.dtype)
    del _x0
    return _d

def reference(L0_attn_x, L0_attn_W_el, L0_attn_b_el, L0_attn_W_le, L0_attn_b_le, L0_ffn_router_w, L0_ffn_w1, L0_ffn_b1, L0_ffn_w2, L0_ffn_b2):

    def _L0_attn_ref(x, W_el, b_el, W_le, b_le):
        import jax, jax.numpy as jnp
        import numpy as np
        _A = np.array([[1, 1, 1, 0, 1, 1, 1, 0, 0, 0, 1, 1], [1, 1, 0, 1, 1, 1, 0, 0, 0, 1, 1, 0], [1, 0, 1, 1, 1, 0, 0, 0, 1, 1, 0, 1], [0, 1, 1, 1, 0, 0, 0, 1, 1, 0, 1, 1], [0, 0, 0, 0, 1, 1, 1, 1, 1, 1, 1, 1], [1, 1, 1, 1, 0, 0, 0, 0, 0, 0, 0, 0], [0, 0, 0, 0, 1, 1, 1, 1, 0, 0, 0, 0], [1, 1, 0, 0, 1, 1, 0, 0, 1, 1, 0, 0], [1, 0, 1, 0, 1, 0, 1, 0, 1, 0, 1, 0], [0, 1, 0, 1, 0, 1, 0, 1, 0, 1, 0, 1], [1, 0, 0, 1, 1, 0, 0, 1, 1, 0, 0, 1], [0, 1, 1, 0, 0, 1, 1, 0, 0, 1, 1, 0]], dtype=np.float32)
        _H = jnp.asarray(np.concatenate([_A.T, np.eye(12, dtype=np.float32)], axis=1))

        def _fractal_dimension(x):
            s = x.reshape(-1)
            sn = (s - s.min()) / (s.max() - s.min() + 1e-10)
            counts = []
            for sc in (2, 4, 8, 16, 32):
                blk = sn[:sc * sc]
                counts.append(jnp.maximum(jnp.sum(blk > blk.mean()).astype(jnp.float32), 1.0))
            lx = jnp.log(jnp.array([2.0, 4.0, 8.0, 16.0, 32.0], dtype=jnp.float32))
            ly = jnp.log(jnp.stack(counts))
            n = jnp.float32(5.0)
            num = n * jnp.sum(lx * ly) - jnp.sum(lx) * jnp.sum(ly)
            den = n * jnp.sum(lx * lx) - jnp.sum(lx) ** 2
            return jnp.clip(-num / den, 1.0, 2.0)

        def _wave_filter(D, d):
            k = jnp.fft.fftfreq(d).astype(jnp.float32)
            ka = jnp.abs(k) + 1e-08
            omega = 1.0 + 0.2 * D
            a = 1.0 + 0.5 * D
            b = 0.1 * D
            real = jnp.sin(omega * D + a * ka)
            phase = omega * D - ka + b * ka ** 2
            return real * jnp.exp(1j * phase)

        def _golay_correct(bits):
            syn = (bits @ _H.T > 0.5).astype(jnp.float32)
            w = syn.sum(-1)
            _, idx = jax.lax.top_k(syn, 3)
            take = (jnp.arange(3)[None, :] < jnp.minimum(w, 3.0)[:, None]).astype(jnp.float32)
            pattern = (jax.nn.one_hot(idx, 24, dtype=jnp.float32) * take[..., None]).sum(axis=1)
            do_fix = ((w > 0) & (w <= 3))[:, None]
            return jnp.where(do_fix, jnp.mod(bits + pattern, 2.0), bits)
        B, S, E = x.shape
        D = _fractal_dimension(x)
        filt = _wave_filter(D, E)
        x1 = jnp.fft.ifft(jnp.fft.fft(x, axis=-1) * filt, axis=-1).real.astype(x.dtype)
        lat = x1 @ W_el + b_el
        bits = (jax.nn.sigmoid(lat) > 0.5).astype(jnp.float32).reshape(B * S, 24)
        corrected = _golay_correct(bits).reshape(B, S, 24)
        return x1 + corrected @ W_le + b_le

    def _L0_ffn_ref(x, router_w, w1, b1, w2, b2):
        import jax, jax.numpy as jnp
        import numpy as np
        B, N, C, F, E, K = (2, 256, 128, 512, 8, 2)
        Bb, Nn, Cc = x.shape
        x_flat = x.reshape(-1, Cc)
        logits = jnp.einsum('tc,ec->te', x_flat, router_w)
        probs = jax.nn.softmax(logits, axis=-1)
        top_w, top_idx = jax.lax.top_k(probs, K)
        top_w = top_w / (jnp.sum(top_w, axis=-1, keepdims=True) + 1e-09)
        h = jnp.einsum('tc,efc->tef', x_flat, w1) + b1[None]
        h = jax.nn.relu(h)
        y = jnp.einsum('tef,ecf->tec', h, w2) + b2[None]
        sel = jnp.take_along_axis(y, top_idx[:, :, None], axis=1)
        out = jnp.einsum('tkc,tk->tc', sel, top_w)
        return out.reshape(Bb, Nn, Cc)
    x = L0_attn_x
    xn = _layernorm(x, axis=-1)
    x = x + _L0_attn_ref(xn, L0_attn_W_el, L0_attn_b_el, L0_attn_W_le, L0_attn_b_le) + _L0_ffn_ref(xn, L0_ffn_router_w, L0_ffn_w1, L0_ffn_b1, L0_ffn_w2, L0_ffn_b2)
    return x

_drawn_inputs = setup_inputs


def setup_inputs(seed=0):
    import zlib

    import numpy as np

    out = dict(_drawn_inputs(seed))
    spreads = {'L0_attn_b_el': (0.0, 0.1),
     'L0_attn_b_le': (0.0, 0.1),
     'L0_ffn_b1': (0.0, 0.1),
     'L0_ffn_b2': (0.0, 0.1)}
    factors = {}
    for name, (base, spread) in spreads.items():
        noise = np.random.default_rng([zlib.crc32(name.encode()), seed]).standard_normal(out[name].shape)
        drawn = base * np.exp(spread * noise) if base else spread * noise
        out[name] = jnp.asarray(drawn.astype(out[name].dtype))
    for name, factor in factors.items():
        out[name] = (out[name] * factor).astype(out[name].dtype)
    return out
```

```python
import concourse.bass as bass
from concourse import mybir
from contextlib import ExitStack
import numpy as np

B, N, C = 32, 256, 128
TOK = B * N
F, E = 512, 8
P = 128
NT = TOK // P
U = 4
TN = U * P
J = NT // U
FC = F // P
NB = 24
LOADS = 4
SCALES = (2, 4, 8, 16, 32)
LX = [float(np.log(np.float32(s))) for s in SCALES]
DEN = 5.0 * sum(v * v for v in LX) - sum(LX) ** 2
PI = float(np.pi)

C_H, C_ID, C_SYN, C_ONE, C_KA, C_KA2, C_LX, C_EIDX, C_ROW1, C_N = 0, 128, 256, 384, 512, 513, 514, 520, 528, 656


def build(nc, x, w_el, b_el, w_le, b_le, rw, w1, b1, w2, b2, cst, out):
    f32, f32r, bf16 = mybir.dt.float32, mybir.dt.float32r, mybir.dt.bfloat16
    ALU, ACT, AX = mybir.AluOpType, mybir.ActivationFunctionType, mybir.AxisListType
    ds = bass.ds

    gt_dram = nc.dram_tensor("gates_by_expert", (NT * E, P), f32, kind="Internal").ap()

    ctx = ExitStack()
    with ctx:
        def sb(name, shape, dt=f32):
            return ctx.enter_context(nc.sbuf_tensor(name, shape, dt))

        def pb(name):
            return ctx.enter_context(nc.psum_tensor(name, [P, 512], f32))

        def sem(name):
            return ctx.enter_context(nc.semaphore(name))

        X = sb("X", [P, NT, C])
        xt_hi = sb("xt_hi", [P, TOK], f32r)
        xt_lo = sb("xt_lo", [P, TOK], f32r)
        w1_hi, w1_lo = sb("w1_hi", [P, E * F], f32r), sb("w1_lo", [P, E * F], f32r)
        w2_hi, w2_lo = sb("w2_hi", [P, E * FC, C], f32r), sb("w2_lo", [P, E * FC, C], f32r)
        ring = sb("ring", [P, 4096])
        h32 = sb("h32", [P, 2, TN])
        stage = sb("stage", [P, 2, 512])
        cs = sb("cs", [P, C_N])
        b1s, b2s = sb("b1s", [P, E * FC]), sb("b2s", [P, E])
        rws, wels, wles = sb("rws", [P, E]), sb("wels", [P, NB]), sb("wles", [NB, C])
        bels, bles = sb("bels", [NB, 1]), sb("bles", [P, 1])
        wle_hi, wle_lo = sb("wle_hi", [NB, C], f32r), sb("wle_lo", [NB, C], f32r)
        syn_w, one_w = sb("syn_w", [NB, P], bf16), sb("one_w", [NB, P], bf16)
        stats = ring[:, 2048:2048 + NT * 6].rearrange("p (t s) -> p t s", s=6)
        mean = sb("mean", [P, NT])
        ve, s0, rstd = sb("ve", [P, NT]), sb("s0", [P, NT]), sb("rstd", [P, NT])
        xn = ring[:, 0:1024].rearrange("p (b u c) -> p b u c", b=2, u=U)
        xt = ring[:, 1024:2048].rearrange("p (b n) -> p b n", b=2)
        ext = sb("ext", [P, 2, J])
        first = ring[0:1, 2048:3072]
        fs = ring[0:1, 3072:4096]
        fr = sb("fr", [P, 32])
        dv = sb("dv", [P, 16])
        hg, mf = sb("hg", [P, C]), sb("mf", [P, C])
        m_hi, m_lo = sb("m_hi", [P, C], f32r), sb("m_lo", [P, C], f32r)
        m2f = sb("m2f", [P, NB])
        m2_hi, m2_lo = sb("m2_hi", [P, P], f32r), sb("m2_lo", [P, P], f32r)
        pr, tk = (h32[:, i, :].rearrange("p (t e) -> p t e", e=E) for i in range(2))
        oh1, gat = (stage[:, i, :].rearrange("p (t e) -> p t e", e=E) for i in range(2))
        r1, r2, r3 = sb("r1", [P, NT]), sb("r2", [P, NT]), sb("r3", [P, NT])
        gt = h32[:, 1, :].rearrange("p (a q) -> p a q", a=4)
        h_hi, h_lo = sb("h_hi", [P, 4, TN], f32r), sb("h_lo", [P, 4, TN], f32r)
        gb = ring[:, 0:2048].rearrange("p (b n) -> p b n", b=4)
        gy, acc, ot = (ring[:, 2048 + i * TN:2048 + (i + 1) * TN] for i in range(3))
        bits, syn, pat = (stage[0:NB, 0, :].bitcast(bf16)[:, 0:TN], stage[0:NB, 0, :].bitcast(bf16)[:, TN:],
                          stage[0:NB, 1, :].bitcast(bf16)[:, 0:TN])
        corr = sb("corr", [NB, TN], f32r)
        ob = ring[:, 3584:4096].rearrange("p (u c) -> p u c", u=U)

        ph = [pb(f"ph{i}") for i in range(4)]
        py = [pb(f"py{i}") for i in range(2)]
        pa, pl = pb("pa"), pb("pl")

        s_x = [sem(f"s_x{i}") for i in range(LOADS)]
        s_cst = sem("s_cst")
        s_small = sem("s_small")
        s_w = [sem(f"s_w{i}") for i in range(2)]
        s_whi = sem("s_whi")
        s_ve = sem("s_ve")
        s_sqrt = sem("s_sqrt")
        s_xn = sem("s_xn")
        s_tr = sem("s_tr")
        s_xt = sem("s_xt")
        s_log = sem("s_log")
        s_split = sem("s_split")
        s_ext = sem("s_ext")
        s_extall = sem("s_extall")
        s_cnt = sem("s_cnt")
        s_ln = sem("s_ln")
        s_D = sem("s_D")
        s_Db = sem("s_Db")
        s_arg = sem("s_arg")
        s_sin = sem("s_sin")
        s_hg = sem("s_hg")
        s_mp = sem("s_mp")
        s_ms = sem("s_ms")
        s_m2p = sem("s_m2p")
        s_m2s = sem("s_m2s")
        s_wts = sem("s_wts")
        s_otp = sem("s_otp")
        s_lx = sem("s_lx")
        s_ex = sem("s_ex")
        s_gat = sem("s_gat")
        s_gtp = sem("s_gtp")
        s_gts = sem("s_gts")
        s_gtd = sem("s_gtd")
        s_gb = [sem(f"s_gb{i}") for i in range(4)]
        s_gbfree = sem("s_gbfree")
        s_h = sem("s_h")
        s_relu = sem("s_relu")
        s_hs = sem("s_hs")
        s_hhi = sem("s_hhi")
        s_pat = sem("s_pat")
        s_y = sem("s_y")
        s_yfree = sem("s_yfree")
        s_lat = sem("s_lat")
        s_bits = sem("s_bits")
        s_synp = sem("s_synp")
        s_syn = sem("s_syn")
        s_wp = sem("s_wp")
        s_corr = sem("s_corr")
        s_a = sem("s_a")
        s_acc = sem("s_acc")
        s_ot = sem("s_ot")
        s_ob = sem("s_ob")
        s_out = sem("s_out")
        s_obfree = sem("s_obfree")
        s_dve = sem("s_dve")

        ident = cs[:, C_ID:C_ID + P]
        WP = 2 * E
        w_src = [w1[:, i * F:(i + 1) * F] for i in range(E)] + [w2[:, i * F:(i + 1) * F] for i in range(E)]
        w_hi = [w1_hi[:, i * F:(i + 1) * F] for i in range(E)] + \
               [w2_hi[:, i * FC:(i + 1) * FC, :].rearrange("p a c -> p (a c)") for i in range(E)]
        w_lo = [w1_lo[:, i * F:(i + 1) * F] for i in range(E)] + \
               [w2_lo[:, i * FC:(i + 1) * FC, :].rearrange("p a c -> p (a c)") for i in range(E)]
        gt_rows = gt_dram.rearrange("(j u e) q -> j e u q", u=U, e=E)
        out_v = out.rearrange("(p t) c -> p t c", p=P)
        x_v = x.rearrange("(p t) c -> p t c", p=P)
        NCH = E * FC
        LAG = 2
        block = ctx.enter_context(nc.Block())

        @block.sync
        def _(sp):
            n = NT // LOADS
            for i in range(LOADS):
                sp.dma_start(X[:, i * n:(i + 1) * n, :], x_v[:, i * n:(i + 1) * n, :]).then_inc(s_x[i], 16)
            for dst, src in ((cs, cst), (rws, rw), (wels, w_el), (wles, w_le), (bels, b_el), (bles, b_le),
                             (b1s, b1), (b2s, b2)):
                sp.dma_start(dst[:, :], src).then_inc(s_small, 16)
            for i in range(WP):
                if i >= 2:
                    sp.wait_ge(s_wts, i - 1)
                sp.dma_start(stage[:, i % 2, :], w_src[i]).then_inc(s_w[i % 2], 16)
            sp.wait_ge(s_gts, 1)
            sp.dma_start(gt_dram.rearrange("(a r) q -> r a q", r=P), gt[:, :, :]).then_inc(s_gtd, 16)
            sp.wait_ge(s_gtd, 16)
            with sp.Fori(0, J) as j:
                for e in range(E):
                    sp.wait_ge(s_yfree, j * E + (e + 1))
                    sp.dma_start(gb[:, e % 4, :].rearrange("p (u q) -> p u q", u=U),
                                 gt_rows[ds(j, 1), e].rearrange("a u q -> (a u) q").partition_broadcast(P))\
                      .then_inc(s_gb[e % 4], 16)

        @block.gpsimd
        def _(pool):
            for i in range(WP):
                pool.wait_ge(s_whi, i + 1)
                nc.gpsimd.tensor_tensor(w_lo[i], stage[:, i % 2, :], w_hi[i], ALU.subtract).then_inc(s_wts, 1)
            pool.sem_inc(s_split, 2)
            with pool.Fori(0, J // 2) as k:
                for b in range(2):
                    pool.wait_ge(s_xt, k * 2 + (b + 3))
                    nc.gpsimd.tensor_tensor(xt_lo[:, ds(k * (2 * TN) + b * TN, TN)], xt[:, b, :],
                                            xt_hi[:, ds(k * (2 * TN) + b * TN, TN)], ALU.subtract)\
                        .then_inc(s_split, 1)
            pool.wait_ge(s_ext, 1)
            nc.gpsimd.partition_all_reduce(fr[:, 2:4], fr[:, 0:2], P, bass.bass_isa.ReduceOp.max).then_inc(s_extall, 1)
            pool.sem_inc(s_obfree, 1)
            with pool.Fori(0, J) as j:
                pool.wait_ge(s_ob, j + 2)
                pool.dma_start(out_v[:, ds(j * U, U), :], ob[:, :, :]).then_inc(s_out, 16)
                pool.wait_ge(s_out, j * 16 + 16)
                pool.sem_inc(s_obfree, 1)
            pool.wait_ge(s_out, 16 * J)

        @block.scalar
        def _(act):
            A = nc.scalar.activation
            for i in range(WP):
                act.wait_ge(s_w[i % 2], 16 * (i // 2 + 1))
                A(w_hi[i], stage[:, i % 2, :], ACT.Copy).then_inc(s_whi, 1)
            act.wait_ge(s_ve, 1)
            A(s0[:, :], ve[:, :], ACT.Sqrt).then_inc(s_sqrt, 1)
            act.sem_inc(s_xt, 2)
            with act.Fori(0, J // 2) as k:
                for b in range(2):
                    act.wait_ge(s_tr, k * 2 + (b + 3))
                    act.wait_ge(s_log, k * 2 + (b + 1))
                    act.wait_ge(s_split, k * 2 + (b + 1))
                    A(xt[:, b, :], ph[b][:, :], ACT.Copy)
                    A(xt_hi[:, ds(k * (2 * TN) + b * TN, TN)], ph[b][:, :], ACT.Copy).then_inc(s_xt, 1)
            act.wait_ge(s_lx, 1)
            A(pr[:, :, :], tk[:, :, :], ACT.Exp).then_inc(s_ex, 1)
            act.wait_ge(s_cnt, 1)
            A(fr[0:1, 16:21], fr[0:1, 8:13], ACT.Ln).then_inc(s_ln, 1)
            act.wait_ge(s_arg, 1)
            A(dv[:, 10:12], dv[:, 8:10], ACT.Sin).then_inc(s_sin, 1)
            act.wait_ge(s_gtp, 1)
            A(gt[:, :, :].rearrange("p a q -> p (a q)"), ph[3][:, :], ACT.Copy).then_inc(s_gts, 1)
            act.wait_ge(s_gtd, 16)
            act.sem_inc(s_relu, 4)
            with act.Fori(0, J) as j:
                for n in range(NCH):
                    act.wait_ge(s_h, j * NCH + (n + 1))
                    act.wait_ge(s_hs, j * NCH + (n + 1))
                    A(h32[:, n % 2, :], ph[n % 4][:, :], ACT.Relu, bias=b1s[:, n:n + 1]).then_inc(s_relu, 1)

        @block.tensor
        def _(pe):
            mm = nc.tensor.matmul
            pe.wait_ge(s_small, 16 * 8)
            pe.sem_inc(s_tr, 2)
            pe.sem_inc(s_log, 2)
            with pe.Fori(0, J // 2) as k:
                for b in range(2):
                    pe.wait_ge(s_xn, k * 2 + (b + 1))
                    pe.wait_ge(s_xt, k * 2 + (b + 1))
                    for u in range(U):
                        last = nc.tensor.transpose(ph[b][:, u * P:(u + 1) * P], xn[:, b, u, :], ident)
                    last.then_inc(s_tr, 1)
                    pe.wait_ge(s_xt, k * 2 + (b + 3))
                    for u in range(U):
                        last = mm(pa[:, ds(k * (2 * U * E) + (b * U + u) * E, E)], xt[:, b, u * P:(u + 1) * P],
                                  rws[:, :], start=True, stop=True)
                    last.then_inc(s_log, 1)
            pe.wait_ge(s_D, 1)
            mm(pl[:, 0:1], cs[0:1, C_ROW1:C_ROW1 + P], fr[0:1, 24:25], start=True, stop=True).then_inc(s_Db, 1)
            pe.wait_ge(s_hg, 1)
            mm(pl[:, 128:256], cs[:, C_H:C_H + P], hg[:, :], start=True, stop=True).then_inc(s_mp, 1)
            pe.wait_ge(s_ms, 1)
            mm(pl[:, 256:256 + NB], mf[:, :], wels[:, :], start=True, stop=True).then_inc(s_m2p, 1)
            pe.wait_ge(s_gat, 1)
            gat2 = gat[:, :, :].rearrange("p t e -> p (t e)")
            for a in range(4):
                last = nc.tensor.transpose(ph[3][:, a * P:(a + 1) * P], gat2[:, a * P:(a + 1) * P], ident)
            last.then_inc(s_gtp, 1)
            pe.wait_ge(s_gts, 1)
            pe.wait_ge(s_m2s, 1)
            pe.wait_ge(s_wts, WP)
            pe.wait_ge(s_split, J + 2)
            pe.sem_inc(s_y, 4)
            with pe.Fori(0, J) as j:
                cols = ds(j * TN, TN)

                def three(o, hi, lo, bhi, blo, start, stop):
                    mm(o, hi, bhi, start=start, stop=False)
                    mm(o, hi, blo, start=False, stop=False)
                    return mm(o, lo, bhi, start=False, stop=stop)

                def up(n):
                    pe.wait_ge(s_relu, j * NCH + (n + 1))
                    w = slice(n * P, (n + 1) * P)
                    three(ph[n % 4][:, :], w1_hi[:, w], w1_lo[:, w], xt_hi[:, cols], xt_lo[:, cols],
                          True, True).then_inc(s_h, 1)

                def down(n):
                    e, c = divmod(n, FC)
                    if c == 0:
                        pe.wait_ge(s_yfree, j * E + (e + 3))
                    pe.wait_ge(s_hs, j * NCH + (n + 3))
                    three(py[e % 2][:, :], w2_hi[:, n, :], w2_lo[:, n, :], h_hi[:, n % 4, :], h_lo[:, n % 4, :],
                          c == 0, c == FC - 1).then_inc(s_y, 1)

                for n in range(NCH):
                    up(n)
                    if n >= LAG:
                        down(n - LAG)
                    if n == 4:
                        pe.wait_ge(s_ob, j + 1)
                        three(pl[:, :], m2_hi[:, :], m2_lo[:, :], xt_hi[:, cols], xt_lo[:, cols],
                              True, True).then_inc(s_lat, 1)
                    if n == 10:
                        pe.wait_ge(s_bits, j + 1)
                        mm(pl[:, :], syn_w[:, :], bits[:, :], start=True, stop=True).then_inc(s_synp, 1)
                    if n == 16:
                        pe.wait_ge(s_syn, j + 1)
                        mm(pl[:, :], one_w[:, :], syn[:, :], start=True, stop=True).then_inc(s_wp, 1)
                    if n == 22:
                        pe.wait_ge(s_corr, j + 1)
                        pe.wait_ge(s_ot, j + 1)
                        three(pa[:, :], m_hi[:, :], m_lo[:, :], xt_hi[:, cols], xt_lo[:, cols], True, False)
                        mm(pa[:, :], wle_hi[:, :], corr[:, :], start=False, stop=False)
                        mm(pa[:, :], wle_lo[:, :], corr[:, :], start=False, stop=True).then_inc(s_a, 1)
                for n in range(NCH - LAG, NCH):
                    down(n)
                pe.wait_ge(s_ot, j + 2)
                for u in range(U):
                    last = nc.tensor.transpose(pl[:, u * P:(u + 1) * P], ot[:, u * P:(u + 1) * P], ident)
                last.then_inc(s_otp, 1)

        @block.vector
        def _(dve):
            V = nc.vector
            steps = [0]

            def mark(ins, times=1):
                steps[0] += times
                return ins.then_inc(s_dve, 1)

            def link(ins):
                mark(ins)
                dve.wait_ge(s_dve, steps[0])

            n = NT // LOADS
            for i in range(LOADS):
                dve.wait_ge(s_x[i], 16)
                with dve.Fori(0, n // U) as k:
                    for u in range(U):
                        t = k * U + (i * n + u)
                        ins = V.bn_stats(stats[:, ds(t, 1), :].rearrange("p a s -> p (a s)"),
                                         X[:, ds(t, 1), :].rearrange("p a c -> p (a c)"))
                    mark(ins, n // U)
            dve.wait_ge(s_dve, steps[0])
            me, qe, mo, qo = (stats[:, :, i] for i in (1, 2, 4, 5))
            V.tensor_tensor(mean[:, :], me, mo, ALU.add)
            V.tensor_tensor(ve[:, :], qe, qo, ALU.add)
            link(V.tensor_tensor(s0[:, :], me, mo, ALU.subtract))
            V.tensor_scalar(mean[:, :], mean[:, :], 0.5, None, ALU.mult)
            V.tensor_scalar(ve[:, :], ve[:, :], 1.0 / C, 1e-5, ALU.mult, ALU.add)
            link(V.tensor_tensor(s0[:, :], s0[:, :], s0[:, :], ALU.mult))
            V.scalar_tensor_tensor(ve[:, :], s0[:, :], 0.25, ve[:, :], ALU.mult, ALU.add).then_inc(s_ve, 1)
            dve.wait_ge(s_sqrt, 1)
            link(V.reciprocal(rstd[:, :], s0[:, :]))
            link(V.tensor_tensor(rstd[:, :], rstd[:, :], ve[:, :], ALU.mult))
            link(V.tensor_tensor(rstd[:, :], rstd[:, :], s0[:, :], ALU.add))
            link(V.tensor_scalar(rstd[:, :], rstd[:, :], 0.5, None, ALU.mult))
            link(V.reciprocal(rstd[:, :], rstd[:, :]))
            with dve.Fori(0, J // 2) as k:
                for b in range(2):
                    dve.wait_ge(s_tr, k * 2 + (b + 1))
                    for u in range(U):
                        t = k * (2 * U) + (b * U + u)
                        ins = V.tensor_scalar(xn[:, b, u, :], X[:, ds(t, 1), :].rearrange("p a c -> p (a c)"),
                                              mean[:, ds(t, 1)], rstd[:, ds(t, 1)], ALU.subtract, ALU.mult)
                    ins.then_inc(s_xn, 1)
                    dve.wait_ge(s_xn, k * 2 + (b + 1))
                    flat = xn[:, b, :, :].rearrange("p u c -> p (u c)")
                    V.tensor_reduce(ext[:, 0, ds(k * 2 + b, 1)], flat, AX.X, ALU.max)
                    ins = V.tensor_reduce(ext[:, 1, ds(k * 2 + b, 1)], flat, AX.X, ALU.min)
                    mark(ins, J // 2)
            dve.wait_ge(s_dve, steps[0])
            V.tensor_reduce(fr[:, 0:1], ext[:, 0, :], AX.X, ALU.max)
            mark(V.tensor_reduce(fr[:, 1:2], ext[:, 1, :], AX.X, ALU.min))
            dve.wait_ge(s_log, J + 2)
            lg = pa[:, :].rearrange("p (t e) -> p t e", e=E)
            link(V.tensor_reduce(r1[:, :], lg, AX.X, ALU.max))
            V.tensor_scalar(fr[:, 1:2], fr[:, 1:2], -1.0, None, ALU.mult).then_inc(s_ext, 1)

            def over_e(a):
                return a[:, :].unsqueeze(2).to_broadcast([P, NT, E])

            V.tensor_tensor(tk[:, :, :], lg, over_e(r1), ALU.subtract).then_inc(s_lx, 1)
            dve.wait_ge(s_ex, 1)
            link(V.tensor_reduce(r1[:, :], pr[:, :, :], AX.X, ALU.add))
            link(V.reciprocal(r1[:, :], r1[:, :]))
            link(V.tensor_tensor(pr[:, :, :], pr[:, :, :], over_e(r1), ALU.mult))
            order = cs[:, C_EIDX:C_EIDX + E].unsqueeze(1).to_broadcast([P, NT, E])
            link(V.tensor_reduce(r1[:, :], pr[:, :, :], AX.X, ALU.max))
            link(V.tensor_tensor(tk[:, :, :], pr[:, :, :], over_e(r1), ALU.is_equal))
            link(V.tensor_tensor(tk[:, :, :], tk[:, :, :], order, ALU.mult))
            link(V.tensor_reduce(r3[:, :], tk[:, :, :], AX.X, ALU.max))
            link(V.tensor_tensor(oh1[:, :, :], tk[:, :, :], over_e(r3), ALU.is_equal))
            link(V.scalar_tensor_tensor(pr[:, :, :], oh1[:, :, :], -2.0, pr[:, :, :], ALU.mult, ALU.add))
            link(V.tensor_reduce(r2[:, :], pr[:, :, :], AX.X, ALU.max))
            link(V.tensor_tensor(tk[:, :, :], pr[:, :, :], over_e(r2), ALU.is_equal))
            link(V.tensor_tensor(tk[:, :, :], tk[:, :, :], order, ALU.mult))
            link(V.tensor_reduce(r3[:, :], tk[:, :, :], AX.X, ALU.max))
            link(V.tensor_tensor(tk[:, :, :], tk[:, :, :], over_e(r3), ALU.is_equal))
            link(V.scalar_tensor_tensor(r3[:, :], r1[:, :], 1e-9, r2[:, :], ALU.add, ALU.add))
            link(V.reciprocal(r3[:, :], r3[:, :]))
            V.tensor_tensor(r1[:, :], r1[:, :], r3[:, :], ALU.mult)
            link(V.tensor_tensor(r2[:, :], r2[:, :], r3[:, :], ALU.mult))
            V.tensor_tensor(oh1[:, :, :], oh1[:, :, :], over_e(r1), ALU.mult)
            link(V.tensor_tensor(tk[:, :, :], tk[:, :, :], over_e(r2), ALU.mult))
            V.tensor_tensor(gat[:, :, :], oh1[:, :, :], tk[:, :, :], ALU.add).then_inc(s_gat, 1)

            n8 = 1024 // C
            f3 = first[:, :].rearrange("p (t c) -> p t c", c=C)
            link(V.tensor_tensor(f3, X[0:1, 0:n8, :], mean[0:1, 0:n8].unsqueeze(2).to_broadcast([1, n8, C]), ALU.subtract))
            link(V.tensor_tensor(f3, f3, rstd[0:1, 0:n8].unsqueeze(2).to_broadcast([1, n8, C]), ALU.mult))
            dve.wait_ge(s_extall, 1)
            link(V.tensor_tensor(fr[0:1, 4:5], fr[0:1, 2:3], fr[0:1, 3:4], ALU.add))
            link(V.tensor_scalar(fr[0:1, 4:5], fr[0:1, 4:5], 1e-10, None, ALU.add))
            link(V.reciprocal(fr[0:1, 5:6], fr[0:1, 4:5]))
            link(V.tensor_scalar(first[:, :], first[:, :], fr[0:1, 3:4], fr[0:1, 5:6], ALU.add, ALU.mult))
            for i, sc in enumerate(SCALES):
                V.tensor_reduce(fr[0:1, 26 + i:27 + i], first[:, 0:sc * sc], AX.X, ALU.add)
            link(V.memset(fr[0:1, 8:13], 0.0))
            for i, sc in enumerate(SCALES):
                last = V.tensor_scalar(fr[0:1, 26 + i:27 + i], fr[0:1, 26 + i:27 + i], 1.0 / (sc * sc), None, ALU.mult)
            link(last)
            for i, sc in enumerate(SCALES):
                last = V.tensor_scalar(fs[:, 0:sc * sc], first[:, 0:sc * sc], fr[0:1, 26 + i:27 + i], None,
                                       ALU.is_gt, ALU.add, accum_out=fr[0:1, 8 + i:9 + i])
                link(last)
            V.tensor_scalar(fr[0:1, 8:13], fr[0:1, 8:13], 1.0, None, ALU.max).then_inc(s_cnt, 1)
            dve.wait_ge(s_ln, 1)
            link(V.tensor_tensor(fr[0:1, 16:21], fr[0:1, 16:21], cs[0:1, C_LX:C_LX + 5], ALU.mult))
            link(V.tensor_reduce(fr[0:1, 25:26], fr[0:1, 16:21], AX.X, ALU.add))
            link(V.tensor_scalar(fr[0:1, 25:26], fr[0:1, 25:26], -1.0 / DEN, 1.0, ALU.mult, ALU.max))
            V.tensor_scalar(fr[0:1, 24:25], fr[0:1, 25:26], 2.0, None, ALU.min).then_inc(s_D, 1)
            dve.wait_ge(s_Db, 1)
            ka, ka2 = cs[:, C_KA:C_KA + 1], cs[:, C_KA2:C_KA2 + 1]
            D, om, a, b = (dv[:, i:i + 1] for i in range(4))
            link(V.tensor_copy(D, pl[:, 0:1]))
            V.tensor_scalar(om, D, 0.2, 1.0, ALU.mult, ALU.add)
            V.tensor_scalar(a, D, 0.5, 1.0, ALU.mult, ALU.add)
            link(V.tensor_scalar(b, D, 0.1, None, ALU.mult))
            V.tensor_tensor(om, om, D, ALU.mult)
            V.tensor_tensor(dv[:, 4:5], a, ka, ALU.mult)
            link(V.tensor_tensor(dv[:, 5:6], b, ka2, ALU.mult))
            V.tensor_tensor(dv[:, 4:5], dv[:, 4:5], om, ALU.add)
            link(V.tensor_tensor(dv[:, 6:7], om, ka, ALU.subtract))
            link(V.tensor_tensor(dv[:, 5:6], dv[:, 5:6], dv[:, 6:7], ALU.add))
            V.tensor_scalar(dv[:, 8:9], dv[:, 4:5], -1.0, PI, ALU.mult, ALU.add)
            V.tensor_scalar(dv[:, 9:10], dv[:, 5:6], -1.0, PI / 2, ALU.mult, ALU.add).then_inc(s_arg, 1)
            dve.wait_ge(s_sin, 1)
            link(V.tensor_tensor(dv[:, 12:13], dv[:, 10:11], dv[:, 11:12], ALU.mult))
            V.tensor_scalar(hg[:, :], cs[:, C_H:C_H + P], dv[:, 12:13], 1.0 / C, ALU.mult, ALU.mult).then_inc(s_hg, 1)
            V.memset(m2_hi[:, :].bitcast(f32), 0.0)
            V.memset(m2_lo[:, :].bitcast(f32), 0.0)
            V.tensor_copy(syn_w[:, :], cs[0:NB, C_SYN:C_SYN + P])
            V.tensor_copy(one_w[:, :], cs[0:NB, C_ONE:C_ONE + P])
            link(V.tensor_copy(wle_hi[:, :], wles[:, :]))
            V.tensor_tensor(wle_lo[:, :], wles[:, :], wle_hi[:, :], ALU.subtract)
            dve.wait_ge(s_mp, 1)
            V.tensor_copy(mf[:, :], pl[:, 128:256]).then_inc(s_ms, 1)
            dve.wait_ge(s_ms, 1)
            link(V.tensor_copy(m_hi[:, :], mf[:, :]))
            link(V.tensor_tensor(m_lo[:, :], mf[:, :], m_hi[:, :], ALU.subtract))
            dve.wait_ge(s_m2p, 1)
            link(V.tensor_copy(m2f[:, :], pl[:, 256:256 + NB]))
            link(V.tensor_copy(m2_hi[:, 0:NB], m2f[:, :]))
            V.tensor_tensor(m2_lo[:, 0:NB], m2f[:, :], m2_hi[:, 0:NB], ALU.subtract).then_inc(s_m2s, 1)

            dve.sem_inc(s_hs, 2)
            dve.sem_inc(s_yfree, 4)
            dve.sem_inc(s_ot, 1)
            dve.sem_inc(s_ob, 1)
            dve.wait_ge(s_gtd, 16)
            base = steps[0]
            with dve.Fori(0, J) as j:
                def gate(e):
                    dve.wait_ge(s_y, j * NCH + ((e + 1) * FC + 4))
                    dve.wait_ge(s_gb[e % 4], j * 32 + 16 * (e // 4 + 1))
                    dst = gy if e else acc
                    V.scalar_tensor_tensor(dst[:, :], py[e % 2][:, :], b2s[:, e:e + 1], gb[:, e % 4, :],
                                           ALU.add, ALU.mult).then_inc(s_yfree, 1)
                    if e:
                        dve.wait_ge(s_yfree, j * E + (e + 5))
                        V.tensor_tensor(acc[:, :], acc[:, :], gy[:, :], ALU.add).then_inc(s_acc, 1)

                for n in range(NCH):
                    dve.wait_ge(s_relu, j * NCH + (n + 5))
                    dve.wait_ge(s_y, j * NCH + (n + 1))
                    V.tensor_copy(h_hi[:, n % 4, :], h32[:, n % 2, :]).then_inc(s_hhi, 1)
                    dve.wait_ge(s_hhi, j * NCH + (n + 1))
                    V.tensor_tensor(h_lo[:, n % 4, :], h32[:, n % 2, :], h_hi[:, n % 4, :],
                                    ALU.subtract).then_inc(s_hs, 1)
                    if n >= FC + 1 and n % FC == 1:
                        gate(n // FC - 1)
                    if n == 7:
                        dve.wait_ge(s_lat, j + 1)
                        V.tensor_scalar(bits[:, :], pl[0:NB, :], bels[:, :], 0.0, ALU.add, ALU.is_gt).then_inc(s_bits, 1)
                    if n == 13:
                        dve.wait_ge(s_synp, j + 1)
                        V.tensor_scalar(syn[:, :], pl[0:NB, :], 0.5, None, ALU.is_gt).then_inc(s_syn, 1)
                    if n == 19:
                        dve.wait_ge(s_wp, j + 1)
                        V.scalar_tensor_tensor(pat[:, :], pl[0:NB, :], 3.0, syn[:, :], ALU.is_le, ALU.mult).then_inc(s_pat, 1)
                        dve.wait_ge(s_pat, j + 1)
                        V.tensor_tensor(corr[:, :], bits[:, :], pat[:, :], ALU.not_equal).then_inc(s_corr, 1)
                gate(E - 1)
                dve.wait_ge(s_a, j + 1)
                dve.wait_ge(s_acc, (j + 1) * (E - 1))
                V.scalar_tensor_tensor(ot[:, :], pa[:, :], bles[:, :], acc[:, :], ALU.add, ALU.add).then_inc(s_ot, 1)
                dve.wait_ge(s_otp, j + 1)
                dve.wait_ge(s_obfree, j + 1)
                V.tensor_tensor(ob[:, :, :].rearrange("p u c -> p (u c)"), pl[:, :],
                                X[:, ds(j * U, U), :].rearrange("p u c -> p (u c)"), ALU.add).then_inc(s_ob, 1)


def kernel(L0_attn_x, L0_attn_W_el, L0_attn_b_el, L0_attn_W_le, L0_attn_b_le, L0_ffn_router_w,
           L0_ffn_w1, L0_ffn_b1, L0_ffn_w2, L0_ffn_b2):
    import concourse.bacc as bacc
    from concourse.bass_utils import run_bass_kernel_spmd

    def lay(a, shape, perm):
        return np.ascontiguousarray(np.asarray(a).reshape(shape).transpose(perm))

    cst = np.zeros((P, C_N), np.float32)
    i = np.arange(P)
    ang = 2 * np.pi * ((i[:, None] * i[None, :]) % P) / P
    cst[:, C_H:C_H + P] = np.cos(ang) + np.sin(ang)
    cst[:, C_ID:C_ID + P] = np.eye(P)
    rows = ("111011100011", "110111000110", "101110001101", "011100011011", "000011111111", "111100000000",
            "000011110000", "110011001100", "101010101010", "010101010101", "100110011001", "011001100110")
    A = np.array([[int(v) for v in r] for r in rows])
    h = np.concatenate([A.T, np.eye(NB // 2)], axis=1)
    cst[0:NB, C_SYN:C_SYN + NB // 2] = h.T
    cst[0:NB, C_ONE:C_ONE + NB] = 1
    ka = (np.abs(np.fft.fftfreq(C).astype(np.float32)) + np.float32(1e-8)).astype(np.float32)
    cst[:, C_KA] = ka
    cst[:, C_KA2] = ka * ka
    cst[:, C_LX:C_LX + 5] = 5 * np.array(LX) - sum(LX)
    cst[:, C_EIDX:C_EIDX + E] = E - np.arange(E)
    cst[:, C_ROW1:C_ROW1 + P] = 1

    arrays = {
        "x": lay(L0_attn_x, (TOK, C), (0, 1)),
        "w_el": lay(L0_attn_W_el, (C, NB), (0, 1)),
        "b_el": lay(L0_attn_b_el, (NB, 1), (0, 1)),
        "w_le": lay(L0_attn_W_le, (NB, C), (0, 1)),
        "b_le": lay(L0_attn_b_le, (C, 1), (0, 1)),
        "rw": lay(L0_ffn_router_w, (E, C), (1, 0)),
        "w1": lay(L0_ffn_w1, (E * F, C), (1, 0)),
        "b1": lay(L0_ffn_b1, (E * FC, P), (1, 0)),
        "w2": np.ascontiguousarray(np.asarray(L0_ffn_w2).reshape(E, C, FC, P).transpose(3, 0, 2, 1)
                                   .reshape(P, E * FC * C)),
        "b2": lay(L0_ffn_b2, (E, C), (1, 0)),
        "cst": cst,
    }
    nc = bacc.Bacc("TRN2", target_bir_lowering=False, num_devices=1, dynamic_dma_scratch_size=8192)
    f32 = mybir.dt.float32
    aps = [nc.dram_tensor("in_" + k, a.shape, f32, kind="ExternalInput").ap() for k, a in arrays.items()]
    out = nc.dram_tensor("out", (TOK, C), f32, kind="ExternalOutput").ap()
    build(nc, *aps, out)
    r = run_bass_kernel_spmd(nc, [{"in_" + k: a for k, a in arrays.items()}], core_ids=[0])
    return r.results[0]["out"].reshape(B, N, C)
```
